# Optimizing a Trainium2 kernel written in Bass

```python
import numpy as np
import jax
import jax.numpy as jnp

def _softmax(x, axis=-1):
    return jax.nn.softmax(x, axis=axis)

def _gelu(x):
    return jax.nn.gelu(x, approximate=True)

def _silu(x):
    return jax.nn.silu(x)

def _sigmoid(x):
    return jax.nn.sigmoid(x)

def _layernorm(x, axis=-1, eps=1e-05):
    m = jnp.mean(x, axis=axis, keepdims=True)
    v = jnp.var(x, axis=axis, keepdims=True)
    return (x - m) / jnp.sqrt(v + eps)

def _scatter_add(tgt, idx, src, axis=0):
    return tgt.at[idx].add(src)

def _segment_sum(src, seg, n):
    return jax.ops.segment_sum(src, seg, n)
kernel_name = 'mk_dlrm_tower_d1_rec_r8_9a555a'

def setup_inputs(seed: int=0):
    np.random.seed(seed)
    _w = jnp.asarray

    def _rec_inputs():
        import jax
        import jax.numpy as jnp
        _tk = jax.random.key(seed)
        ids = jnp.stack([jax.random.randint(jax.random.fold_in(_tk, 200 + f), (512,), 0, v, jnp.int32) for f, v in enumerate([125000, 1000, 12500, 12500, 1250, 1000, 1250, 12500, 1000, 1000, 1000, 1250, 1000, 1000, 1000, 12500, 1000, 12500, 1250, 1000, 1250, 12500, 12500, 1250, 1250, 1000])], axis=1)
        tbl_0 = 0.05 * jax.random.normal(jax.random.fold_in(_tk, 500 + 0), (125000, 128), jnp.float32)
        tbl_1 = 0.05 * jax.random.normal(jax.random.fold_in(_tk, 500 + 1), (1000, 128), jnp.float32)
        tbl_2 = 0.05 * jax.random.normal(jax.random.fold_in(_tk, 500 + 2), (12500, 128), jnp.float32)
        tbl_3 = 0.05 * jax.random.normal(jax.random.fold_in(_tk, 500 + 3), (12500, 128), jnp.float32)
        tbl_4 = 0.05 * jax.random.normal(jax.random.fold_in(_tk, 500 + 4), (1250, 128), jnp.float32)
        tbl_5 = 0.05 * jax.random.normal(jax.random.fold_in(_tk, 500 + 5), (1000, 128), jnp.float32)
        tbl_6 = 0.05 * jax.random.normal(jax.random.fold_in(_tk, 500 + 6), (1250, 128), jnp.float32)
        tbl_7 = 0.05 * jax.random.normal(jax.random.fold_in(_tk, 500 + 7), (12500, 128), jnp.float32)
        tbl_8 = 0.05 * jax.random.normal(jax.random.fold_in(_tk, 500 + 8), (1000, 128), jnp.float32)
        tbl_9 = 0.05 * jax.random.normal(jax.random.fold_in(_tk, 500 + 9), (1000, 128), jnp.float32)
        tbl_10 = 0.05 * jax.random.normal(jax.random.fold_in(_tk, 500 + 10), (1000, 128), jnp.float32)
        tbl_11 = 0.05 * jax.random.normal(jax.random.fold_in(_tk, 500 + 11), (1250, 128), jnp.float32)
        tbl_12 = 0.05 * jax.random.normal(jax.random.fold_in(_tk, 500 + 12), (1000, 128), jnp.float32)
        tbl_13 = 0.05 * jax.random.normal(jax.random.fold_in(_tk, 500 + 13), (1000, 128), jnp.float32)
        tbl_14 = 0.05 * jax.random.normal(jax.random.fold_in(_tk, 500 + 14), (1000, 128), jnp.float32)
        tbl_15 = 0.05 * jax.random.normal(jax.random.fold_in(_tk, 500 + 15), (12500, 128), jnp.float32)
        tbl_16 = 0.05 * jax.random.normal(jax.random.fold_in(_tk, 500 + 16), (1000, 128), jnp.float32)
        tbl_17 = 0.05 * jax.random.normal(jax.random.fold_in(_tk, 500 + 17), (12500, 128), jnp.float32)
        tbl_18 = 0.05 * jax.random.normal(jax.random.fold_in(_tk, 500 + 18), (1250, 128), jnp.float32)
        tbl_19 = 0.05 * jax.random.normal(jax.random.fold_in(_tk, 500 + 19), (1000, 128), jnp.float32)
        tbl_20 = 0.05 * jax.random.normal(jax.random.fold_in(_tk, 500 + 20), (1250, 128), jnp.float32)
        tbl_21 = 0.05 * jax.random.normal(jax.random.fold_in(_tk, 500 + 21), (12500, 128), jnp.float32)
        tbl_22 = 0.05 * jax.random.normal(jax.random.fold_in(_tk, 500 + 22), (12500, 128), jnp.float32)
        tbl_23 = 0.05 * jax.random.normal(jax.random.fold_in(_tk, 500 + 23), (1250, 128), jnp.float32)
        tbl_24 = 0.05 * jax.random.normal(jax.random.fold_in(_tk, 500 + 24), (1250, 128), jnp.float32)
        tbl_25 = 0.05 * jax.random.normal(jax.random.fold_in(_tk, 500 + 25), (1000, 128), jnp.float32)
        _rk = jax.random.fold_in(_tk, 7)
        r_dense_x = -0.000514642 + 1.00011 * jax.random.normal(jax.random.fold_in(_rk, 101), (512, 128), jnp.float32)
        W_top1 = 0.0456912 * jax.random.normal(jax.random.fold_in(_tk, 801), (479, 512), jnp.float32)
        W_top2 = 0.0441942 * jax.random.normal(jax.random.fold_in(_tk, 802), (512, 256), jnp.float32)
        W_top3 = 0.0625 * jax.random.normal(jax.random.fold_in(_tk, 803), (256, 1), jnp.float32)
        b_top1 = jnp.zeros((512,), jnp.float32)
        b_top2 = jnp.zeros((256,), jnp.float32)
        return (r_dense_x, ids, tbl_0, tbl_1, tbl_2, tbl_3, tbl_4, tbl_5, tbl_6, tbl_7, tbl_8, tbl_9, tbl_10, tbl_11, tbl_12, tbl_13, tbl_14, tbl_15, tbl_16, tbl_17, tbl_18, tbl_19, tbl_20, tbl_21, tbl_22, tbl_23, tbl_24, tbl_25, W_top1, b_top1, W_top2, b_top2, W_top3)
    r_dense_x, ids, tbl_0, tbl_1, tbl_2, tbl_3, tbl_4, tbl_5, tbl_6, tbl_7, tbl_8, tbl_9, tbl_10, tbl_11, tbl_12, tbl_13, tbl_14, tbl_15, tbl_16, tbl_17, tbl_18, tbl_19, tbl_20, tbl_21, tbl_22, tbl_23, tbl_24, tbl_25, W_top1, b_top1, W_top2, b_top2, W_top3 = _rec_inputs()

    def _L0_rec_setup():
        import jax, jax.numpy as jnp
        import numpy as np
        F = 26
        D = 128
        B = 2048
        _TRIU_I, _TRIU_J = np.triu_indices(F + 1, k=1)
        _TRIU_I = jnp.asarray(_TRIU_I)
        _TRIU_J = jnp.asarray(_TRIU_J)
        key = jax.random.key(seed)
        k1, k2 = jax.random.split(key)
        sparse_x = jax.random.normal(k1, (B, F, D), dtype=jnp.float32)
        dense_x = jax.random.normal(k2, (B, D), dtype=jnp.float32)
        return {'sparse_x': sparse_x, 'dense_x': dense_x}
    _L0_rec_all = _L0_rec_setup()
    _L0_rec_in = {k: v for k, v in _L0_rec_all.items() if k in ()}
    del _L0_rec_all
    return {'r_dense_x': r_dense_x, 'ids': ids, 'tbl_0': tbl_0, 'tbl_1': tbl_1, 'tbl_2': tbl_2, 'tbl_3': tbl_3, 'tbl_4': tbl_4, 'tbl_5': tbl_5, 'tbl_6': tbl_6, 'tbl_7': tbl_7, 'tbl_8': tbl_8, 'tbl_9': tbl_9, 'tbl_10': tbl_10, 'tbl_11': tbl_11, 'tbl_12': tbl_12, 'tbl_13': tbl_13, 'tbl_14': tbl_14, 'tbl_15': tbl_15, 'tbl_16': tbl_16, 'tbl_17': tbl_17, 'tbl_18': tbl_18, 'tbl_19': tbl_19, 'tbl_20': tbl_20, 'tbl_21': tbl_21, 'tbl_22': tbl_22, 'tbl_23': tbl_23, 'tbl_24': tbl_24, 'tbl_25': tbl_25, 'W_top1': W_top1, 'b_top1': b_top1, 'W_top2': W_top2, 'b_top2': b_top2, 'W_top3': W_top3}

def reference(r_dense_x, ids, tbl_0, tbl_1, tbl_2, tbl_3, tbl_4, tbl_5, tbl_6, tbl_7, tbl_8, tbl_9, tbl_10, tbl_11, tbl_12, tbl_13, tbl_14, tbl_15, tbl_16, tbl_17, tbl_18, tbl_19, tbl_20, tbl_21, tbl_22, tbl_23, tbl_24, tbl_25, W_top1, b_top1, W_top2, b_top2, W_top3):
    import jax
    import jax.numpy as jnp

    def _L0_rec_ref(sparse_x, dense_x):
        import jax, jax.numpy as jnp
        import numpy as np
        F = 26
        D = 128
        B = 2048
        _TRIU_I, _TRIU_J = np.triu_indices(F + 1, k=1)
        _TRIU_I = jnp.asarray(_TRIU_I)
        _TRIU_J = jnp.asarray(_TRIU_J)
        combined = jnp.concatenate([sparse_x, dense_x[:, None, :]], axis=1)
        interact = jnp.einsum('bfd,bgd->bfg', combined, combined)
        return interact[:, _TRIU_I, _TRIU_J]
    e = jnp.stack([tbl_0[ids[:, 0]], tbl_1[ids[:, 1]], tbl_2[ids[:, 2]], tbl_3[ids[:, 3]], tbl_4[ids[:, 4]], tbl_5[ids[:, 5]], tbl_6[ids[:, 6]], tbl_7[ids[:, 7]], tbl_8[ids[:, 8]], tbl_9[ids[:, 9]], tbl_10[ids[:, 10]], tbl_11[ids[:, 11]], tbl_12[ids[:, 12]], tbl_13[ids[:, 13]], tbl_14[ids[:, 14]], tbl_15[ids[:, 15]], tbl_16[ids[:, 16]], tbl_17[ids[:, 17]], tbl_18[ids[:, 18]], tbl_19[ids[:, 19]], tbl_20[ids[:, 20]], tbl_21[ids[:, 21]], tbl_22[ids[:, 22]], tbl_23[ids[:, 23]], tbl_24[ids[:, 24]], tbl_25[ids[:, 25]]], axis=1)
    z = _L0_rec_ref(e, r_dense_x)
    z = z.reshape(z.shape[0], -1)
    h = jnp.concatenate([z, r_dense_x], axis=1)
    h = jnp.maximum(h @ W_top1 + b_top1, 0.0)
    h = jnp.maximum(h @ W_top2 + b_top2, 0.0)
    y = h @ W_top3
    return y

_drawn_inputs = setup_inputs


def setup_inputs(seed=0):
    import zlib

    import numpy as np

    out = dict(_drawn_inputs(seed))
    spreads = {'b_top1': (0.0, 0.1), 'b_top2': (0.0, 0.1)}
    factors = {}
    for name, (base, spread) in spreads.items():
        noise = np.random.default_rng([zlib.crc32(name.encode()), seed]).standard_normal(out[name].shape)
        drawn = base * np.exp(spread * noise) if base else spread * noise
        out[name] = jnp.asarray(drawn.astype(out[name].dtype))
    for name, factor in factors.items():
        out[name] = (out[name] * factor).astype(out[name].dtype)
    return out
```

```python
from contextlib import ExitStack

import concourse.bass as bass
from concourse import mybir

P = 128
B = 512
D = 128
NTAB = 26
F = NTAB + 1
PAIRS = F * (F - 1) // 2
N1, N2 = 512, 256

TILES = B // P
SLOTS = 4
FP = P // SLOTS
Q = P // SLOTS
QB = 4
GB = Q // QB
BANK = 512
ZC = 3
ZK = PAIRS // ZC
C1, C2 = N1 // P, N2 // P
GROUPS = [range(0, 4), range(4, 8), range(8, 12), range(12, 16), range(16, 20), range(20, 24), range(24, 27)]
NG = len(GROUPS)


def build(nc, dense, ids, tables, W1, b1, W2, b2, W3, y):
    fp32 = mybir.dt.float32
    u32 = mybir.dt.uint32
    ALU = mybir.AluOpType
    ACT = mybir.ActivationFunctionType

    with ExitStack() as ctx:
        def sb(name, shape, dt=fp32):
            return ctx.enter_context(nc.sbuf_tensor(name, shape, dt))

        def ps(name, shape):
            return ctx.enter_context(nc.psum_tensor(name, shape, fp32))

        def sem(name):
            return ctx.enter_context(nc.semaphore(name))

        ids_sb = sb("ids_sb", [P, TILES, NTAB], mybir.dt.int32)
        rows = sb("rows", [P, TILES, NTAB, D])
        dense_sb = sb("dense_sb", [P, TILES, D])
        ident = sb("ident", [P, P])
        featT = sb("featT", [P, 2, Q, SLOTS, FP])
        denseT = sb("denseT", [P, TILES, P])
        gram = sb("gram", [P, TILES, F, Q])
        gramT = sb("gramT", [P, TILES, F, FP])
        z = sb("z", [P, TILES, PAIRS])
        zT = sb("zT", [ZK, ZC, TILES, P])
        w1z = sb("w1z", [ZK, ZC, N1])
        w1d = sb("w1d", [D, N1])
        w2 = sb("w2", [P, C1, N2])
        w3 = sb("w3", [P, C2])
        b1c = sb("b1c", [P, C1])
        b2c = sb("b2c", [P, C2])
        h1T = sb("h1T", [P, TILES, C1, P])
        h2T = sb("h2T", [P, TILES, C2, P])
        y_row = sb("y_row", [1, P, TILES])

        ps_tp = [ps(f"ps_tp{i}", [P, 4, P]) for i in range(2)]
        ps_gram = [ps(f"ps_gram{i}", [P, BANK]) for i in range(2)]
        ps_z = ps("ps_z", [P, ZC, P])
        ps_h1 = ps("ps_h1", [P, C1, P])
        ps_h2 = ps("ps_h2", [P, C2, P])
        ps_y = ps("ps_y", [1, TILES, P])

        ids_in = sem("ids_in")
        dense_in = sem("dense_in")
        w1_in = sem("w1_in")
        w2_in = sem("w2_in")
        small_in = sem("small_in")
        ident_zero = sem("ident_zero")
        ident_ready = sem("ident_ready")
        rows_in = [[sem(f"rows_in_{t}_{g}") for g in range(NG)] for t in range(TILES)]
        pad_ready = sem("pad_ready")
        tp_done = sem("tp_done")
        tp_used = sem("tp_used")
        gram_done = sem("gram_done")
        gram_act = sem("gram_act")
        gram_dve = sem("gram_dve")
        gramT_done = sem("gramT_done")
        z_done = sem("z_done")
        ztp_done = sem("ztp_done")
        zT_done = sem("zT_done")
        h1_done = sem("h1_done")
        h1_relu = sem("h1_relu")
        h2_done = sem("h2_done")
        h2_relu = sem("h2_relu")
        y_done = sem("y_done")
        y_copied = sem("y_copied")
        y_out = sem("y_out")

        block = ctx.enter_context(nc.Block())

        @block.sync
        def _(sp):
            sp.dma_start(ids_sb[:, :, :], ids.rearrange("(p t) f -> p t f", t=TILES)).then_inc(ids_in, 16)
            sp.dma_start(dense_sb[:, :, :], dense.rearrange("(p t) d -> p t d", t=TILES)).then_inc(dense_in, 16)
            sp.dma_start(w1z[:, :, :], W1[0:PAIRS, :].rearrange("(c k) n -> k c n", c=ZC)).then_inc(w1_in, 16)
            sp.dma_start(w1d[:, :], W1[PAIRS:PAIRS + D, :]).then_inc(w1_in, 16)
            sp.dma_start(w2[:, :, :], W2.rearrange("(c p) n -> p c n", p=P)).then_inc(w2_in, 16)
            with nc.allow_non_contiguous_dma(reason="three short vectors laid along the partitions"):
                sp.dma_start(b1c[:, :], b1.rearrange("(c p) -> p c", p=P)).then_inc(small_in, 16)
                sp.dma_start(b2c[:, :], b2.rearrange("(c p) -> p c", p=P)).then_inc(small_in, 16)
                sp.dma_start(w3[:, :], W3.rearrange("(c p) o -> p (c o)", p=P)).then_inc(small_in, 16)
            sp.wait_ge(y_copied, 1)
            sp.dma_start(y.rearrange("(a b) o -> a (b o)", a=1), y_row[:, :, :].rearrange("a p t -> a (p t)")
                         ).then_inc(y_out, 16)
            sp.wait_ge(y_out, 16)

        @block.gpsimd
        def _(pool):
            nc.gpsimd.memset(ident[:, :], 0.0).then_inc(ident_zero, 1)
            pool.wait_ge(ident_zero, 1)
            nc.gpsimd.affine_select(out=ident[:, :], in_=ident[:, :], compare_op=ALU.not_equal, fill=1.0,
                                    base=0, pattern=[[-1, P]], channel_multiplier=1).then_inc(ident_ready, 1)
            pool.wait_ge(ids_in, 16)
            for t in range(TILES):
                for g, group in enumerate(GROUPS):
                    for f in group:
                        if f < NTAB:
                            pool.indirect_dma_start(
                                out=rows[:, t, f, :], out_offset=None, in_=tables[f],
                                in_offset=bass.IndirectOffsetOnAxis(ap=ids_sb[:, t, f:f + 1].bitcast(u32), axis=0),
                            ).then_inc(rows_in[t][g], 16)

        @block.tensor
        def _(pe):
            def transpose_group(t, g):
                n = t * NG + g
                pe.wait_ge(rows_in[t][g], 16 * len([f for f in GROUPS[g] if f < NTAB]))
                if n >= 2:
                    pe.wait_ge(tp_used, n - 1)
                for k, f in enumerate(GROUPS[g]):
                    src = rows[:, t, f, :] if f < NTAB else dense_sb[:, t, :]
                    last = nc.tensor.transpose(ps_tp[n % 2][:, k, :], src, ident[:, :])
                last.then_inc(tp_done, 1)

            def gram_tile(t):
                pe.wait_ge(tp_used, (t + 1) * NG)
                if t == 0:
                    pe.wait_ge(pad_ready, 1)
                for g in range(GB):
                    n = t * GB + g
                    if n >= 2:
                        pe.wait_ge(gram_act, n - 1)
                        pe.wait_ge(gram_dve, n - 1)
                    for k in range(QB):
                        q = g * QB + k
                        last = nc.tensor.matmul(ps_gram[n % 2][:, k * SLOTS * F:(k + 1) * SLOTS * F],
                                                featT[:, t % 2, q, :, :].rearrange("d s f -> d (s f)"),
                                                featT[:, t % 2, q, :, 0:F], start=True, stop=True)
                    last.then_inc(gram_done, 1)

            def transpose_z(t):
                pe.wait_ge(z_done, 26 * (t + 1))
                if t >= 1:
                    pe.wait_ge(zT_done, t)
                for c in range(ZC):
                    last = nc.tensor.transpose(ps_z[0:ZK, c, :], z[:, t, c * ZK:(c + 1) * ZK], ident[:, :])
                last.then_inc(ztp_done, 1)

            def layer1(t):
                pe.wait_ge(zT_done, t + 1)
                if t == 0:
                    pe.wait_ge(w1_in, 32)
                else:
                    pe.wait_ge(h1_relu, C1 * t)
                for n in range(C1):
                    nc.tensor.matmul(ps_h1[:, n, :], w1d[:, n * P:(n + 1) * P], denseT[:, t, :],
                                     start=True, stop=False)
                    for c in range(ZC):
                        last = nc.tensor.matmul(ps_h1[:, n, :], w1z[:, c, n * P:(n + 1) * P], zT[:, c, t, :],
                                                start=False, stop=c == ZC - 1)
                last.then_inc(h1_done, 1)

            def layer2(t):
                pe.wait_ge(h1_relu, C1 * (t + 1))
                if t == 0:
                    pe.wait_ge(w2_in, 16)
                else:
                    pe.wait_ge(h2_relu, C2 * t)
                for n in range(C2):
                    for c in range(C1):
                        last = nc.tensor.matmul(ps_h2[:, n, :], w2[:, c, n * P:(n + 1) * P], h1T[:, t, c, :],
                                                start=c == 0, stop=c == C1 - 1)
                last.then_inc(h2_done, 1)

            def layer3(t):
                pe.wait_ge(h2_relu, C2 * (t + 1))
                if t == 0:
                    pe.wait_ge(small_in, 48)
                for c in range(C2):
                    last = nc.tensor.matmul(ps_y[0:1, t, :], w3[:, c:c + 1], h2T[:, t, c, :],
                                            start=c == 0, stop=c == C2 - 1)
                last.then_inc(y_done, 1)

            pe.wait_ge(ident_ready, 1)
            pe.wait_ge(dense_in, 16)
            after = {1: transpose_z, 3: layer1, 4: layer2, 5: layer3}
            for t in range(TILES):
                for g in range(NG):
                    transpose_group(t, g)
                    if t >= 1 and g in after:
                        after[g](t - 1)
                gram_tile(t)
            for step in after.values():
                step(TILES - 1)

        @block.scalar
        def _(act):
            def copy_group(t, g):
                n = t * NG + g
                act.wait_ge(tp_done, n + 1)
                if t >= 2 and g == 0:
                    act.wait_ge(gram_done, (t - 1) * GB)
                f0, m = GROUPS[g][0], len(GROUPS[g])
                out = featT[:, t % 2, :, :, f0:f0 + m].rearrange("d q s f -> d f s q")
                if g == NG - 1:
                    nc.scalar.copy(denseT[:, t, :], ps_tp[n % 2][:, m - 1, :])
                nc.scalar.copy(out, ps_tp[n % 2][:, 0:m, :].rearrange("d f (s q) -> d f s q", q=Q)).then_inc(tp_used, 1)

            def copy_gram(t):
                for g in range(GB):
                    n = t * GB + g
                    act.wait_ge(gram_done, n + 1)
                    for s in (0, 1):
                        src = ps_gram[n % 2][s * FP:(s + 1) * FP, 0:QB * SLOTS * F].rearrange(
                            "i (q s j) -> i s j q", q=QB, s=SLOTS)[:, s]
                        last = nc.scalar.copy(gram[s * FP:(s + 1) * FP, t, :, g * QB:(g + 1) * QB], src)
                    last.then_inc(gram_act, 1)

            def relu1(t):
                if t == 0:
                    act.wait_ge(small_in, 48)
                act.wait_ge(h1_done, t + 1)
                for n in range(C1):
                    nc.scalar.activation(h1T[:, t, n, :], ps_h1[:, n, :], ACT.Relu,
                                         bias=b1c[:, n:n + 1]).then_inc(h1_relu, 1)

            def relu2(t):
                act.wait_ge(h2_done, t + 1)
                for n in range(C2):
                    nc.scalar.activation(h2T[:, t, n, :], ps_h2[:, n, :], ACT.Relu,
                                         bias=b2c[:, n:n + 1]).then_inc(h2_relu, 1)

            after = {3: relu1, 4: relu2}
            for t in range(TILES):
                for g in range(NG):
                    copy_group(t, g)
                    if t >= 1 and g in after:
                        after[g](t - 1)
                copy_gram(t)
            for step in after.values():
                step(TILES - 1)

        @block.vector
        def _(dve):
            nc.vector.memset(featT[:, :, :, :, F:FP], 0.0).then_inc(pad_ready, 1)
            for t in range(TILES):
                for g in range(GB):
                    n = t * GB + g
                    dve.wait_ge(gram_done, n + 1)
                    for s in (2, 3):
                        src = ps_gram[n % 2][s * FP:(s + 1) * FP, 0:QB * SLOTS * F].rearrange(
                            "i (q s j) -> i s j q", q=QB, s=SLOTS)[:, s]
                        last = nc.vector.tensor_copy(gram[s * FP:(s + 1) * FP, t, :, g * QB:(g + 1) * QB], src)
                    last.then_inc(gram_dve, 1)
                dve.wait_ge(gram_act, (t + 1) * GB)
                dve.wait_ge(gram_dve, (t + 1) * GB)
                nc.vector.transpose(gramT[:, t, :, :].rearrange("b j i -> b (j i)"),
                                    gram[:, t, :, :].rearrange("p j q -> p (j q)")).then_inc(gramT_done, 1)
                dve.wait_ge(gramT_done, t + 1)
                off = 0
                for i in range(F - 1):
                    m = F - 1 - i
                    nc.vector.tensor_copy(z[:, t, off:off + m], gramT[:, t, i, i + 1:F]).then_inc(z_done, 1)
                    off += m
                dve.wait_ge(ztp_done, t + 1)
                nc.vector.tensor_copy(zT[:, :, t, :], ps_z[0:ZK, :, :]).then_inc(zT_done, 1)
            dve.wait_ge(y_done, TILES)
            nc.vector.tensor_copy(y_row[:, :, :], ps_y[:, :, :].rearrange("a t p -> a p t")).then_inc(y_copied, 1)


_INS = ["r_dense_x", "ids"] + [f"tbl_{i}" for i in range(NTAB)] + ["W_top1", "b_top1", "W_top2", "b_top2", "W_top3"]


def kernel(**inputs):
    import numpy as _np
    import concourse.bacc as _bacc
    from concourse import mybir as _mybir
    from concourse.bass_utils import run_bass_kernel_spmd as _run

    nc = _bacc.Bacc("TRN2", target_bir_lowering=False, num_devices=1)
    arrays, aps = {}, []
    for name in _INS:
        a = _np.ascontiguousarray(inputs[name])
        arrays[f"in_{name}"] = a
        aps.append(nc.dram_tensor(f"in_{name}", a.shape, _mybir.dt.from_np(a.dtype), kind="ExternalInput").ap())
    y = nc.dram_tensor("out_y", (B, 1), _mybir.dt.float32, kind="ExternalOutput").ap()
    dense, ids = aps[0:2]
    W1, b1, W2, b2, W3 = aps[2 + NTAB:]
    build(nc, dense, ids, aps[2:2 + NTAB], W1, b1, W2, b2, W3, y)
    r = _run(nc, [arrays], core_ids=[0])
    return r.results[0]["out_y"]
```

```python
from contextlib import ExitStack

import concourse.bass as bass
from concourse import mybir

P = 128
B = 512
D = 128
NTAB = 26
F = NTAB + 1
DENSE = NTAB
PAIRS = F * (F - 1) // 2
N1, N2 = 512, 256

TILES = B // P
S = 32
SLOTS = P // S
GW = SLOTS * F
QB = 4
GB = S // QB
BANK = 512
ZC = 3
ZK = PAIRS // ZC
C1, C2 = N1 // P, N2 // P

LOOKUP = [1, 5, 8, 9, 10, 12, 13, 14]
NL = len(LOOKUP)
VOC = 1000
VC = 8
VK = VOC // VC
VM = VK // 16 * 16
VA = 2
VD = (VC - VA) // 2
RAW = 3
ROWB = 3

GATHER = [f for f in range(NTAB) if f not in LOOKUP]
NGA = len(GATHER)
GROUPS = [(GATHER + [DENSE])[i:i + 4] for i in range(0, NGA + 1, 4)]
NG = len(GROUPS)

_groups = [("group", _t, _g) for _t in range(2) for _g in range(NG)]
FILLS = []
for _k in range(NL):
    FILLS += [("table", _k)]
    FILLS += [_groups.pop(0)] if _k >= 1 else []
FILLS += _groups
START = len(FILLS)
FILLS += [("group", _t, _g) for _t in range(2, TILES) for _g in range(NG)]
FILL_NR = {fill: n for n, fill in enumerate(FILLS)}


def runs(group):
    out = []
    for k, f in enumerate(group):
        if out and out[-1][1] + out[-1][2] == f:
            out[-1][2] += 1
        else:
            out.append([k, f, 1])
    return out


def build(nc, dense, ids, tables, W1, b1, W2, b2, W3, y):
    fp32 = mybir.dt.float32
    fp32r = mybir.dt.float32r
    u32 = mybir.dt.uint32
    i32 = mybir.dt.int32
    ALU = mybir.AluOpType
    ACT = mybir.ActivationFunctionType

    with ExitStack() as ctx:
        def sb(name, shape, dt=fp32):
            return ctx.enter_context(nc.sbuf_tensor(name, shape, dt))

        def ps(name, shape):
            return ctx.enter_context(nc.psum_tensor(name, shape, fp32))

        def sem(name):
            return ctx.enter_context(nc.semaphore(name))

        ids_sb = sb("ids_sb", [P, TILES, NTAB], i32)
        ids_r = sb("ids_r", [P, TILES, NTAB], fp32r)
        rows = sb("rows", [P, ROWB, NGA, D])
        dense_sb = sb("dense_sb", [P, TILES, D])
        ident = sb("ident", [P, P])
        ident_r = sb("ident_r", [P, P], fp32r)
        vnr_i = sb("vnr_i", [P, VC], i32)
        vnr = sb("vnr", [P, VC])
        table_raw = sb("table_raw", [VK, RAW, VC, D])
        table_hi = sb("table_hi", [VK, 2, VC, D], fp32r)
        table_lo = sb("table_lo", [VK, 2, VC, D], fp32r)
        onehot = sb("onehot", [VK, 2, VC, B], fp32r)
        featT = sb("featT", [P, TILES, S, SLOTS, S])
        denseT = sb("denseT", [P, TILES, P])
        gram = sb("gram", [P, 2, F, S])
        gramT = sb("gramT", [P, F, S])
        ids_act = sb("ids_act", [VK, B])
        away = sb("away", [VK, VA, B])
        z = sb("z", [P, 2, PAIRS])
        zT = sb("zT", [ZK, ZC, 2, P])
        w1z = sb("w1z", [ZK, ZC, N1])
        w1d = sb("w1d", [D, N1])
        w2 = sb("w2", [P, C1, N2])
        w3 = sb("w3", [P, C2])
        b1c = sb("b1c", [P, C1])
        b2c = sb("b2c", [P, C2])
        h1T = sb("h1T", [P, 2, C1, P])
        h2T = sb("h2T", [P, 2, C2, P])
        y_row = sb("y_row", [1, P, TILES])

        ps_tp = [ps(f"ps_tp{i}", [P, 4, P]) for i in range(2)]
        ps_gram = [ps(f"ps_gram{i}", [P, BANK]) for i in range(2)]
        ps_zy = ps("ps_zy", [P, ZC + 1, P])
        ps_h1 = [ps(f"ps_h1{i}", [P, TILES, P]) for i in range(2)]
        ps_h2 = ps("ps_h2", [P, BANK // P, P])

        ids_in = sem("ids_in")
        dense_in = sem("dense_in")
        w1_in = sem("w1_in")
        w2_in = sem("w2_in")
        small_in = sem("small_in")
        raw_in = [sem(f"raw_in_{i}") for i in range(RAW)]
        ident_zero = sem("ident_zero")
        ident_ready = sem("ident_ready")
        vnr_ready = sem("vnr_ready")
        rows_in = [[sem(f"rows_in_{t}_{g}") for g in range(NG)] for t in range(TILES)]
        pad_ready = sem("pad_ready")
        consts_ready = sem("consts_ready")
        hi_done = sem("hi_done")
        lo_done = sem("lo_done")
        ids_bc = sem("ids_bc")
        ids_copied = sem("ids_copied")
        onehot_dve = sem("onehot_dve")
        away_done = sem("away_done")
        warm_done = sem("warm_done")
        onehot_act = sem("onehot_act")
        fill_done = sem("fill_done")
        fill_used = sem("fill_used")
        gram_done = sem("gram_done")
        gram_act = sem("gram_act")
        gram_dve = sem("gram_dve")
        gramT_done = sem("gramT_done")
        z_done = sem("z_done")
        ztp_done = sem("ztp_done")
        zT_done = sem("zT_done")
        h1_done = sem("h1_done")
        h1_relu = sem("h1_relu")
        h2_done = sem("h2_done")
        h2_relu = sem("h2_relu")
        y_done = sem("y_done")
        y_copied = sem("y_copied")
        y_out = sem("y_out")

        block = ctx.enter_context(nc.Block())

        @block.sync
        def _(sp):
            def load_table(k):
                src = tables[LOOKUP[k]].rearrange("(k c) d -> k c d", c=VC)
                if k >= RAW:
                    sp.wait_ge(hi_done, k - RAW + 1)
                    sp.wait_ge(lo_done, k - RAW + 1)
                sp.dma_start(table_raw[0:VM, k % RAW], src[0:VM]).then_inc(raw_in[k % RAW], 16)
                sp.dma_start(table_raw[VM:VK, k % RAW], src[VM:VK]).then_inc(raw_in[k % RAW], 16)

            sp.dma_start(ids_sb[:, :, :], ids.rearrange("(p t) f -> p t f", t=TILES)).then_inc(ids_in, 16)
            for k in range(RAW):
                load_table(k)
            sp.dma_start(dense_sb[:, :, :], dense.rearrange("(p t) d -> p t d", t=TILES)).then_inc(dense_in, 16)
            for k in range(RAW, NL):
                load_table(k)
            sp.dma_start(w1z[:, :, :], W1[0:PAIRS, :].rearrange("(c k) n -> k c n", c=ZC)).then_inc(w1_in, 16)
            sp.dma_start(w1d[:, :], W1[PAIRS:PAIRS + D, :]).then_inc(w1_in, 16)
            sp.dma_start(w2[:, :, :], W2.rearrange("(c p) n -> p c n", p=P)).then_inc(w2_in, 16)
            with nc.allow_non_contiguous_dma(reason="three short vectors laid along the partitions"):
                sp.dma_start(b1c[:, :], b1.rearrange("(c p) -> p c", p=P)).then_inc(small_in, 16)
                sp.dma_start(b2c[:, :], b2.rearrange("(c p) -> p c", p=P)).then_inc(small_in, 16)
                sp.dma_start(w3[:, :], W3.rearrange("(c p) o -> p (c o)", p=P)).then_inc(small_in, 16)
            sp.wait_ge(y_copied, TILES)
            sp.dma_start(y.rearrange("(a b) o -> a (b o)", a=1), y_row[:, :, :].rearrange("a p t -> a (p t)")
                         ).then_inc(y_out, 16)
            sp.wait_ge(y_out, 16)

        @block.gpsimd
        def _(pool):
            nc.gpsimd.memset(ident[:, :], 0.0).then_inc(ident_zero, 1)
            nc.gpsimd.iota(vnr_i[:, :], pattern=[[1, VC]], base=0, channel_multiplier=VC).then_inc(vnr_ready, 1)
            pool.wait_ge(ident_zero, 1)
            nc.gpsimd.affine_select(out=ident[:, :], in_=ident[:, :], compare_op=ALU.not_equal, fill=1.0,
                                    base=0, pattern=[[-1, P]], channel_multiplier=1).then_inc(ident_ready, 1)
            nc.gpsimd.memset(featT[:, :, :, :, F:S], 0.0).then_inc(pad_ready, 1)
            pool.wait_ge(ids_in, 16)
            for t in range(TILES):
                if t >= ROWB:
                    pool.wait_ge(fill_done, FILL_NR[("group", t - ROWB, NG - 1)] + 1)
                for n, f in enumerate(GATHER):
                    pool.indirect_dma_start(
                        out=rows[:, t % ROWB, n, :], out_offset=None, in_=tables[f],
                        in_offset=bass.IndirectOffsetOnAxis(ap=ids_sb[:, t, f:f + 1].bitcast(u32), axis=0),
                    ).then_inc(rows_in[t][n // 4], 16)

        @block.tensor
        def _(pe):
            def fill_bank(fill):
                n = FILL_NR[fill]
                if n >= 2:
                    pe.wait_ge(fill_used, n - 1)
                return ps_tp[n % 2]

            def broadcast_ids(k):
                f = LOOKUP[k]
                for t in range(TILES):
                    last = nc.tensor.matmul(ps_h1[k % 2][:, t, :], ids_r[:, t, f:f + 1].broadcast_to([P, P]),
                                            ident_r[:, :], start=True, stop=True)
                last.then_inc(ids_bc, 1)

            def lookup(k):
                bank = fill_bank(("table", k))
                pe.wait_ge(hi_done, k + 1)
                pe.wait_ge(lo_done, k + 1)
                for c in range(VC):
                    if c in (0, VD):
                        pe.wait_ge(onehot_dve, 2 * k + c // VD + 1)
                    if c == VD and k + 2 < NL:
                        pe.wait_ge(ids_copied, k + 1)
                        broadcast_ids(k + 2)
                    if c >= 2 * VD:
                        pe.wait_ge(onehot_act, VA * k + c - 2 * VD + 1)
                    for part in (table_hi, table_lo):
                        last = nc.tensor.matmul(bank[:, :, :], part[:, k % 2, c, :], onehot[:, k % 2, c, :],
                                                start=c == 0 and part is table_hi,
                                                stop=c == VC - 1 and part is table_lo)
                last.then_inc(fill_done, 1)

            def transpose_group(t, g):
                bank = fill_bank(("group", t, g))
                pe.wait_ge(rows_in[t][g], 16 * len([f for f in GROUPS[g] if f != DENSE]))
                for k, f in enumerate(GROUPS[g]):
                    if f == DENSE and t == 0:
                        pe.wait_ge(dense_in, 16)
                    src = dense_sb[:, t, :] if f == DENSE else rows[:, t % ROWB, 4 * g + k, :]
                    last = nc.tensor.transpose(bank[:, k, :], src, ident[:, :])
                last.then_inc(fill_done, 1)

            def gram_banks(t, banks):
                if banks[0] == 0:
                    pe.wait_ge(fill_used, max(START, FILL_NR[("group", t, NG - 1)] + 1))
                    if t == 0:
                        pe.wait_ge(pad_ready, 1)
                for g in banks:
                    n = t * GB + g
                    if n >= 2:
                        pe.wait_ge(gram_act, n - 1)
                        pe.wait_ge(gram_dve, n - 1)
                    for k in range(QB):
                        q = g * QB + k
                        last = nc.tensor.matmul(ps_gram[n % 2][:, k * GW:(k + 1) * GW],
                                                featT[:, t, q, :, :].rearrange("d s f -> d (s f)"),
                                                featT[:, t, q, :, 0:F], start=True, stop=True)
                    last.then_inc(gram_done, 1)

            def transpose_z(t):
                pe.wait_ge(z_done, (F - 1) * (t + 1))
                if t >= 1:
                    pe.wait_ge(y_copied, min(t, TILES - 2))
                for c in range(ZC):
                    last = nc.tensor.transpose(ps_zy[0:ZK, c, :], z[:, t % 2, c * ZK:(c + 1) * ZK], ident[:, :])
                last.then_inc(ztp_done, 1)

            def layer1(t):
                pe.wait_ge(zT_done, t + 1)
                if t == 0:
                    pe.wait_ge(w1_in, 32)
                else:
                    pe.wait_ge(h1_relu, C1 * t)
                for n in range(C1):
                    bank = ps_h1[n // 2][:, n % 2, :]
                    nc.tensor.matmul(bank, w1d[:, n * P:(n + 1) * P], denseT[:, t, :],
                                     start=True, stop=False)
                    for c in range(ZC):
                        last = nc.tensor.matmul(bank, w1z[:, c, n * P:(n + 1) * P], zT[:, c, t % 2, :],
                                                start=False, stop=c == ZC - 1)
                    if n % 2 == 1:
                        last.then_inc(h1_done, 1)

            def layer2(t):
                pe.wait_ge(h1_relu, C1 * (t + 1))
                if t == 0:
                    pe.wait_ge(w2_in, 16)
                else:
                    pe.wait_ge(h2_relu, C2 * t)
                for n in range(C2):
                    for c in range(C1):
                        last = nc.tensor.matmul(ps_h2[:, n, :], w2[:, c, n * P:(n + 1) * P],
                                                h1T[:, t % 2, c, :], start=c == 0, stop=c == C1 - 1)
                last.then_inc(h2_done, 1)

            def layer3(t):
                pe.wait_ge(h2_relu, C2 * (t + 1))
                if t == 0:
                    pe.wait_ge(small_in, 48)
                else:
                    pe.wait_ge(y_copied, t)
                for c in range(C2):
                    last = nc.tensor.matmul(ps_zy[0:1, ZC, :], w3[:, c:c + 1], h2T[:, t % 2, c, :],
                                            start=c == 0, stop=c == C2 - 1)
                last.then_inc(y_done, 1)

            pe.wait_ge(consts_ready, 3)
            broadcast_ids(0)
            broadcast_ids(1)
            pe.wait_ge(ident_ready, 1)
            for fill in FILLS[:START]:
                if fill[0] == "table":
                    lookup(fill[1])
                else:
                    transpose_group(*fill[1:])
            gram_banks(0, range(GB))
            gram_banks(1, range(0, 4))
            transpose_z(0)
            gram_banks(1, range(4, GB))
            for t in range(2, TILES):
                layer1(t - 2)
                for g in range(NG):
                    transpose_group(t, g)
                layer2(t - 2)
                gram_banks(t, range(0, 2))
                layer3(t - 2)
                gram_banks(t, range(2, 4))
                transpose_z(t - 1)
                gram_banks(t, range(4, GB))
            layer1(TILES - 2)
            transpose_z(TILES - 1)
            layer2(TILES - 2)
            layer1(TILES - 1)
            layer3(TILES - 2)
            layer2(TILES - 1)
            layer3(TILES - 1)

        @block.scalar
        def _(act):
            def split_hi(k):
                act.wait_ge(raw_in[k % RAW], 32 * (k // RAW + 1))
                if k >= 2:
                    act.wait_ge(fill_done, FILL_NR[("table", k - 2)] + 1)
                nc.scalar.copy(table_hi[:, k % 2], table_raw[:, k % RAW]).then_inc(hi_done, 1)

            def copy_ids(k):
                act.wait_ge(ids_bc, k + 1)
                if k >= 1:
                    act.wait_ge(away_done, VA * k)
                nc.scalar.copy(ids_act[:, :], ps_h1[k % 2][0:VK, :, :].rearrange("k t p -> k (t p)")
                               ).then_inc(ids_copied, 1)

            def write_away(k):
                act.wait_ge(ids_copied, k + 1)
                if k >= 1:
                    act.wait_ge(onehot_act, VA * k)
                for a in range(VA):
                    nc.scalar.activation(away[:, a, :], ids_act[:, :], ACT.Abs, scale=-1.0,
                                         bias=vnr[0:VK, VC - VA + a:VC - VA + a + 1]).then_inc(away_done, 1)

            def write_onehot(k):
                if k >= 2:
                    act.wait_ge(fill_done, FILL_NR[("table", k - 2)] + 1)
                for a in range(VA):
                    act.wait_ge(away_done, VA * k + a + 1)
                    nc.scalar.activation(onehot[:, k % 2, VC - VA + a, :], away[:, a, :], ACT.Relu, scale=-1.0,
                                         bias=1.0).then_inc(onehot_act, 1)

            def copy_table(k):
                n = FILL_NR[("table", k)]
                f = LOOKUP[k]
                act.wait_ge(fill_done, n + 1)
                nc.scalar.copy(featT[:, :, :, :, f].rearrange("d t q s -> d t s q"),
                               ps_tp[n % 2][:, :, :].rearrange("d t (s q) -> d t s q", q=S)).then_inc(fill_used, 1)

            def copy_group(t, g):
                n = FILL_NR[("group", t, g)]
                act.wait_ge(fill_done, n + 1)
                if GROUPS[g][-1] == DENSE:
                    nc.scalar.copy(denseT[:, t, :], ps_tp[n % 2][:, len(GROUPS[g]) - 1, :])
                for k, f, m in runs(GROUPS[g]):
                    last = nc.scalar.copy(featT[:, t, :, :, f:f + m].rearrange("d q s f -> d f s q"),
                                          ps_tp[n % 2][:, k:k + m, :].rearrange("d f (s q) -> d f s q", q=S))
                last.then_inc(fill_used, 1)

            def copy_gram(t, banks):
                if t >= 2:
                    act.wait_ge(gramT_done, t - 1)
                for g in banks:
                    n = t * GB + g
                    act.wait_ge(gram_done, n + 1)
                    for s in (0, 1):
                        src = ps_gram[n % 2][s * S:(s + 1) * S, 0:QB * GW].rearrange(
                            "i (q s j) -> i s j q", q=QB, s=SLOTS)[:, s]
                        last = nc.scalar.copy(gram[s * S:(s + 1) * S, t % 2, :, g * QB:(g + 1) * QB], src)
                    last.then_inc(gram_act, 1)

            def copy_fill(fill):
                if fill[0] == "table":
                    copy_table(fill[1])
                else:
                    copy_group(*fill[1:])

            def relu1(t):
                if t == 0:
                    act.wait_ge(small_in, 48)
                for n in range(C1):
                    if n % 2 == 0:
                        act.wait_ge(h1_done, 2 * t + n // 2 + 1)
                    nc.scalar.activation(h1T[:, t % 2, n, :], ps_h1[n // 2][:, n % 2, :], ACT.Relu,
                                         bias=b1c[:, n:n + 1]).then_inc(h1_relu, 1)

            def relu2(t):
                act.wait_ge(h2_done, t + 1)
                for n in range(C2):
                    nc.scalar.activation(h2T[:, t % 2, n, :], ps_h2[:, n, :], ACT.Relu,
                                         bias=b2c[:, n:n + 1]).then_inc(h2_relu, 1)

            def copy_fill(fill):
                if fill[0] == "table":
                    copy_table(fill[1])
                else:
                    copy_group(*fill[1:])

            act.wait_ge(consts_ready, 1)
            nc.scalar.activation(away[0:VK, 0, 0:VC], vnr[0:VK, :], ACT.Abs).then_inc(warm_done, 1)
            act.wait_ge(warm_done, 1)
            act.wait_ge(consts_ready, 3)
            copy_ids(0)
            write_away(0)
            write_onehot(0)
            split_hi(0)
            split_hi(1)
            copy_ids(1)
            for k in range(1, NL):
                write_away(k)
                copy_table(k - 1)
                if k + 1 < NL:
                    split_hi(k + 1)
                    copy_ids(k + 1)
                for fill in FILLS[FILL_NR[("table", k - 1)] + 1:FILL_NR[("table", k)]]:
                    copy_fill(fill)
                write_onehot(k)
            for fill in FILLS[FILL_NR[("table", NL - 1)]:START]:
                copy_fill(fill)
            copy_gram(0, range(GB))
            copy_gram(1, range(GB))
            for t in range(2, TILES):
                relu1(t - 2)
                for g in range(NG):
                    copy_group(t, g)
                relu2(t - 2)
                copy_gram(t, range(GB))
            relu1(TILES - 2)
            relu2(TILES - 2)
            relu1(TILES - 1)
            relu2(TILES - 1)

        @block.vector
        def _(dve):
            def split_lo(k):
                dve.wait_ge(hi_done, k + 1)
                if k >= 2:
                    dve.wait_ge(fill_done, FILL_NR[("table", k - 2)] + 1)
                nc.vector.tensor_tensor(table_lo[:, k % 2], table_raw[:, k % RAW], table_hi[:, k % 2].bitcast(fp32),
                                        ALU.subtract).then_inc(lo_done, 1)

            def write_onehot(k):
                dve.wait_ge(ids_copied, k + 1)
                if k >= 2:
                    dve.wait_ge(fill_done, FILL_NR[("table", k - 2)] + 1)
                for c in (0, VD):
                    nc.vector.tensor_tensor(
                        onehot[:, k % 2, c:c + VD, :],
                        ps_h1[k % 2][0:VK, :, :].rearrange("k t (o p) -> k o (t p)", o=1).broadcast_to([VK, VD, B]),
                        vnr[0:VK, c:c + VD].rearrange("k (c o) -> k c o", o=1).broadcast_to([VK, VD, B]),
                        ALU.is_equal).then_inc(onehot_dve, 1)

            def copy_gram(t, banks):
                for g in banks:
                    n = t * GB + g
                    dve.wait_ge(gram_done, n + 1)
                    if g == 0 and t >= 2:
                        dve.wait_ge(gramT_done, t - 1)
                    for s in (2, 3):
                        src = ps_gram[n % 2][s * S:(s + 1) * S, 0:QB * GW].rearrange(
                            "i (q s j) -> i s j q", q=QB, s=SLOTS)[:, s]
                        last = nc.vector.tensor_copy(gram[s * S:(s + 1) * S, t % 2, :, g * QB:(g + 1) * QB], src)
                    last.then_inc(gram_dve, 1)

            def transpose_gram(t):
                dve.wait_ge(gram_act, (t + 1) * GB)
                dve.wait_ge(gram_dve, (t + 1) * GB)
                if t >= 1:
                    dve.wait_ge(z_done, (F - 1) * t)
                nc.vector.transpose(gramT[:, :, :].rearrange("b j i -> b (j i)"),
                                    gram[:, t % 2, :, :].rearrange("p j q -> p (j q)")).then_inc(gramT_done, 1)

            def pack_pairs(t, features):
                dve.wait_ge(gramT_done, t + 1)
                if t >= 2:
                    dve.wait_ge(ztp_done, t - 1)
                for i in features:
                    at, n = i * (2 * F - i - 1) // 2, F - 1 - i
                    nc.vector.tensor_copy(z[:, t % 2, at:at + n], gramT[:, i, i + 1:F]).then_inc(z_done, 1)

            def copy_zT(t):
                dve.wait_ge(ztp_done, t + 1)
                if t >= 2:
                    dve.wait_ge(h1_done, 2 * (t - 1))
                nc.vector.tensor_copy(zT[:, :, t % 2, :], ps_zy[0:ZK, 0:ZC, :]).then_inc(zT_done, 1)

            def copy_y(t):
                dve.wait_ge(y_done, t + 1)
                nc.vector.tensor_copy(y_row[:, :, t], ps_zy[0:1, ZC, :]).then_inc(y_copied, 1)

            dve.wait_ge(vnr_ready, 1)
            nc.vector.tensor_copy(vnr[:, :], vnr_i[:, :]).then_inc(consts_ready, 1)
            dve.wait_ge(ident_ready, 1)
            nc.vector.tensor_copy(ident_r[:, :], ident[:, :]).then_inc(consts_ready, 1)
            dve.wait_ge(ids_in, 16)
            nc.vector.tensor_copy(ids_r[:, :, :], ids_sb[:, :, :]).then_inc(consts_ready, 1)
            dve.wait_ge(consts_ready, 3)
            write_onehot(0)
            split_lo(0)
            for k in range(1, NL):
                split_lo(k)
                write_onehot(k)
            copy_gram(0, range(GB))
            transpose_gram(0)
            for t in range(1, TILES):
                copy_gram(t, range(0, 2))
                if t == 1:
                    pack_pairs(0, range(0, 8))
                else:
                    copy_y(t - 2)
                copy_gram(t, range(2, 3))
                if t == 1:
                    pack_pairs(0, range(8, 17))
                copy_gram(t, range(3, 4))
                if t == 1:
                    pack_pairs(0, range(17, F - 1))
                copy_zT(t - 1)
                copy_gram(t, range(4, GB))
                transpose_gram(t)
                pack_pairs(t, range(F - 1))
            copy_zT(TILES - 1)
            copy_y(TILES - 2)
            copy_y(TILES - 1)


_INS = ["r_dense_x", "ids"] + [f"tbl_{i}" for i in range(NTAB)] + ["W_top1", "b_top1", "W_top2", "b_top2", "W_top3"]


def kernel(**inputs):
    import numpy as _np
    import concourse.bacc as _bacc
    from concourse import mybir as _mybir
    from concourse.bass_utils import run_bass_kernel_spmd as _run

    nc = _bacc.Bacc("TRN2", target_bir_lowering=False, num_devices=1)
    arrays, aps = {}, []
    for name in _INS:
        a = _np.ascontiguousarray(inputs[name])
        arrays[f"in_{name}"] = a
        aps.append(nc.dram_tensor(f"in_{name}", a.shape, _mybir.dt.from_np(a.dtype), kind="ExternalInput").ap())
    y = nc.dram_tensor("out_y", (B, 1), _mybir.dt.float32, kind="ExternalOutput").ap()
    dense, ids = aps[0:2]
    W1, b1, W2, b2, W3 = aps[2 + NTAB:]
    build(nc, dense, ids, aps[2:2 + NTAB], W1, b1, W2, b2, W3, y)
    r = _run(nc, [arrays], core_ids=[0])
    return r.results[0]["out_y"]
```

```python
from contextlib import ExitStack

import concourse.bass as bass
from concourse import mybir

P = 128
B = 512
D = 128
NTAB = 26
F = NTAB + 1
DENSE = NTAB
PAIRS = F * (F - 1) // 2
N1, N2 = 512, 256

TILES = B // P
S = 32
SLOTS = P // S
FJ = F - 1
GW = SLOTS * FJ
GM = (SLOTS - 1) * S + FJ
QB = 4
GB = S // QB
BANK = 512
ZC = 3
ZK = PAIRS // ZC
C1, C2 = N1 // P, N2 // P

LOOKUP = [1, 5, 8, 9, 10, 12, 13, 14]
NL = len(LOOKUP)
EARLY = 3
FULL = NL - 1
LATER_T = 2
VOC = 1000
VC = 8
VK = VOC // VC
VM = VK // 16 * 16
ACHUNKS = [2] * (FULL - 1) + [3, 2]
ABEFORE = [sum(ACHUNKS[:_k]) for _k in range(NL + 1)]
VD = 3
RAW = 3
WARM = (4, 15)
ROWB = 3

GATHER = [f for f in range(NTAB) if f not in LOOKUP[:FULL]]
NGA = len(GATHER)
GROUPS = [([DENSE] + GATHER)[_n:min(_n + 4, NGA)] for _n in range(0, NGA, 4)]
GROUPS += [GATHER[-1:]]
NG = len(GROUPS)


def group_of(t, g):
    return [f for f in GROUPS[g] if t < LATER_T or f not in LOOKUP]


def first_tile(k):
    return 0 if k < FULL else LATER_T


AFTER_TABLE = [[] if _k == 0 else [_k - 1] for _k in range(FULL)] + [[]]
BEFORE = sum(AFTER_TABLE, [])[-1] + 1
LATER = list(range(BEFORE, 2 * NG))
LATER_BANKS = [GB * (_k + 1) // (len(LATER) + 1) for _k in range(len(LATER))]
assert NG <= BEFORE
AHEAD = 2


def features_up_to(c):
    return next(n for n in range(F) if n * (2 * F - n - 1) // 2 >= (c + 1) * ZK)


APACK = features_up_to(0)
APACK_MORE = 4
PPACK = 6
DPACK = F - 1 - APACK - APACK_MORE - PPACK


def runs(group):
    out = []
    for k, f in enumerate(group):
        if out and out[-1][1] + out[-1][2] == f:
            out[-1][2] += 1
        else:
            out.append([k, f, 1])
    return out


def build(nc, dense, ids, tables, W1, b1, W2, b2, W3, y):
    fp32 = mybir.dt.float32
    fp32r = mybir.dt.float32r
    u32 = mybir.dt.uint32
    i32 = mybir.dt.int32
    ALU = mybir.AluOpType
    ACT = mybir.ActivationFunctionType

    with ExitStack() as ctx:
        def sb(name, shape, dt=fp32):
            return ctx.enter_context(nc.sbuf_tensor(name, shape, dt))

        def ps(name, shape):
            return ctx.enter_context(nc.psum_tensor(name, shape, fp32))

        def sem(name):
            return ctx.enter_context(nc.semaphore(name))

        ids_sb = sb("ids_sb", [P, TILES, NTAB], i32)
        ids_r = sb("ids_r", [P, TILES, NTAB], fp32r)
        idsT = sb("idsT", [NTAB, B], fp32r)
        rows = sb("rows", [P, ROWB, NGA, D])
        dense_sb = sb("dense_sb", [P, TILES, D])
        ident = sb("ident", [P, P])
        ident_r = sb("ident_r", [P, P], fp32r)
        vnr_i = sb("vnr_i", [P, VC], i32)
        vnr = sb("vnr", [P, VC])
        table_raw = sb("table_raw", [VK, RAW, VC, D])
        table_hi = sb("table_hi", [VK, 2, VC, D], fp32r)
        table_lo = sb("table_lo", [VK, 2, VC, D], fp32r)
        onehot = sb("onehot", [VK, 2, VC, B], fp32r)
        featT = sb("featT", [P, TILES, S, SLOTS, S])
        denseT = sb("denseT", [P, TILES, P])
        gram = sb("gram", [P, 2, FJ, S])
        gramT = sb("gramT", [P, FJ, S])
        away = sb("away", [VK, ACHUNKS[FULL - 1] + ACHUNKS[NL - 1], B])
        z = sb("z", [P, 2, PAIRS])
        zT = sb("zT", [ZK, ZC, 2, P])
        w1z = sb("w1z", [ZK, ZC, N1])
        w1d = sb("w1d", [D, N1])
        w2 = sb("w2", [P, C1, N2])
        w3 = sb("w3", [P, C2])
        b1c = sb("b1c", [P, C1])
        b2c = sb("b2c", [P, C2])
        h1T = sb("h1T", [P, 2, C1, P])
        h2T = sb("h2T", [P, 2, C2, P])
        y_row = sb("y_row", [1, P, TILES])

        ps_tp = [ps(f"ps_tp{i}", [P, 4, P]) for i in range(2)]
        ps_gram = [ps(f"ps_gram{i}", [P, BANK]) for i in range(2)]
        ps_z = ps("ps_z", [P, BANK // P, P])
        ps_h1 = [ps(f"ps_h1{i}", [P, TILES, P]) for i in range(2)]
        last_z = [ps_tp[0][0:ZK, 0, :], ps_z[0:ZK, 1, :], ps_gram[0][0:ZK, 0:P]]
        ps_h2 = [ps("ps_h2", [P, BANK // P, P])] * (TILES - 1) + [ps_tp[1]]
        table_bank = [ps_gram[k % 2] for k in range(FULL)] + [ps_h2[0][:, :, :].rearrange("d t p -> d (t p)")]

        ids_in = sem("ids_in")
        dense_in = sem("dense_in")
        w1_in = sem("w1_in")
        w2_in = sem("w2_in")
        small_in = sem("small_in")
        raw_in = [sem(f"raw_in_{i}") for i in range(RAW)]
        ident_zero = sem("ident_zero")
        ident_ready = sem("ident_ready")
        vnr_ready = sem("vnr_ready")
        rows_in = [[sem(f"rows_in_{t}_{g}") for g in range(NG)] for t in range(TILES)]
        pad_ready = sem("pad_ready")
        rim_ready = sem("rim_ready")
        consts_ready = sem("consts_ready")
        hi_done = sem("hi_done")
        lo_done = sem("lo_done")
        ids_bc = sem("ids_bc")
        idsT_done = sem("idsT_done")
        idsT_ready = sem("idsT_ready")
        onehot_dve = sem("onehot_dve")
        away_done = sem("away_done")
        warm_done = sem("warm_done")
        onehot_act = sem("onehot_act")
        table_done = sem("table_done")
        table_used = sem("table_used")
        group_done = sem("group_done")
        group_used = sem("group_used")
        gram_done = sem("gram_done")
        gram_act = sem("gram_act")
        gram_dve = sem("gram_dve")
        gramT_done = sem("gramT_done")
        z_done = sem("z_done")
        z_pool = sem("z_pool")
        z_act = sem("z_act")
        ztp_done = sem("ztp_done")
        zT_done = sem("zT_done")
        ztp_last = sem("ztp_last")
        zT_first = sem("zT_first")
        h1_done = sem("h1_done")
        h1_relu = sem("h1_relu")
        h2_done = sem("h2_done")
        h2_relu = sem("h2_relu")
        y_done = sem("y_done")
        y_copied = sem("y_copied")
        y_out = sem("y_out")

        block = ctx.enter_context(nc.Block())

        @block.sync
        def _(sp):
            def load_table(k):
                src = tables[LOOKUP[k]].rearrange("(k c) d -> k c d", c=VC)
                if k >= RAW:
                    sp.wait_ge(hi_done, k - RAW + 1)
                    sp.wait_ge(lo_done, k - RAW + 1)
                sp.dma_start(table_raw[0:VM, k % RAW], src[0:VM]).then_inc(raw_in[k % RAW], 16)
                sp.dma_start(table_raw[VM:VK, k % RAW], src[VM:VK]).then_inc(raw_in[k % RAW], 16)

            sp.dma_start(ids_sb[:, :, :], ids.rearrange("(p t) f -> p t f", t=TILES)).then_inc(ids_in, 16)
            for k in range(RAW):
                load_table(k)
            sp.dma_start(dense_sb[:, :, :], dense.rearrange("(p t) d -> p t d", t=TILES)).then_inc(dense_in, 16)
            for k in range(RAW, NL):
                load_table(k)
            sp.dma_start(w1z[:, :, :], W1[0:PAIRS, :].rearrange("(c k) n -> k c n", c=ZC)).then_inc(w1_in, 16)
            sp.dma_start(w1d[:, :], W1[PAIRS:PAIRS + D, :]).then_inc(w1_in, 16)
            sp.dma_start(w2[:, :, :], W2.rearrange("(c p) n -> p c n", p=P)).then_inc(w2_in, 16)
            with nc.allow_non_contiguous_dma(reason="three short vectors laid along the partitions"):
                sp.dma_start(b1c[:, :], b1.rearrange("(c p) -> p c", p=P)).then_inc(small_in, 16)
                sp.dma_start(b2c[:, :], b2.rearrange("(c p) -> p c", p=P)).then_inc(small_in, 16)
                sp.dma_start(w3[:, :], W3.rearrange("(c p) o -> p (c o)", p=P)).then_inc(small_in, 16)
            sp.wait_ge(y_copied, TILES)
            sp.dma_start(y.rearrange("(a b) o -> a (b o)", a=1), y_row[:, :, :].rearrange("a p t -> a (p t)")
                         ).then_inc(y_out, 16)
            sp.wait_ge(y_out, 16)

        @block.gpsimd
        def _(pool):
            nc.gpsimd.memset(ident[:, :], 0.0).then_inc(ident_zero, 1)
            nc.gpsimd.iota(vnr_i[:, :], pattern=[[1, VC]], base=0, channel_multiplier=VC).then_inc(vnr_ready, 1)
            pool.wait_ge(ident_zero, 1)
            nc.gpsimd.affine_select(out=ident[:, :], in_=ident[:, :], compare_op=ALU.not_equal, fill=1.0,
                                    base=0, pattern=[[-1, P]], channel_multiplier=1).then_inc(ident_ready, 1)
            pool.wait_ge(ident_ready, 1)
            nc.gpsimd.memset(gram[P - S:P, :, :, :], 0.0).then_inc(rim_ready, 1)
            pool.wait_ge(ids_in, 16)
            group_nr = {f: g for g, group in enumerate(GROUPS) for f in group}
            for t in range(TILES):
                if t >= ROWB:
                    pool.wait_ge(group_done, NG * (t - ROWB + 1))
                for n, f in enumerate(GATHER):
                    if f not in group_of(t, group_nr[f]):
                        continue
                    pool.indirect_dma_start(
                        out=rows[:, t % ROWB, n, :], out_offset=None, in_=tables[f],
                        in_offset=bass.IndirectOffsetOnAxis(ap=ids_sb[:, t, f:f + 1].bitcast(u32), axis=0),
                    ).then_inc(rows_in[t][group_nr[f]], 16)

            t = TILES - 1
            pool.wait_ge(gramT_done, 2 * (t + 1))
            pool.wait_ge(ztp_done, t - 1)
            for j in range(F - 1 - PPACK, F - 1):
                at = j * (2 * F - j - 1) // 2
                nc.gpsimd.tensor_copy(z[:, t % 2, at:at + F - 1 - j], gramT[:, j, j:FJ]).then_inc(z_pool, 1)

        @block.tensor
        def _(pe):
            def keep_busy(count):
                for _ in range(count):
                    nc.tensor.matmul(ps_z[:, :, :], ident_r[:, :],
                                     ident_r[:, :].rearrange("k (o p) -> k o p", o=1).broadcast_to([P, BANK // P, P]),
                                     start=True, stop=True)

            def broadcast_ids(k):
                f = LOOKUP[k]
                t = first_tile(k)
                if k < EARLY:
                    for t in range(TILES):
                        last = nc.tensor.matmul(ps_h1[k % 2][:, t, :], ids_r[:, t, f:f + 1].broadcast_to([P, P]),
                                                ident_r[:, :], start=True, stop=True)
                else:
                    pe.wait_ge(idsT_ready, 1)
                    last = nc.tensor.matmul(ps_h1[k % 2][0:VK, t:TILES, :].rearrange("k t p -> k (t p)"),
                                            ident_r[0:NTAB, f:f + 1].broadcast_to([NTAB, VK]), idsT[:, t * P:B],
                                            start=True, stop=True)
                last.then_inc(ids_bc, 1)

            def lookup(k):
                if 2 <= k < FULL:
                    pe.wait_ge(table_used, k - 1)
                at = first_tile(k) * P
                pe.wait_ge(hi_done, k + 1)
                pe.wait_ge(lo_done, k + 1)
                for c in range(VC):
                    if c in (0, VD):
                        pe.wait_ge(onehot_dve, 2 * k + c // VD + 1)
                    if c == VD and k + 2 < NL:
                        pe.wait_ge(away_done, ABEFORE[max(k, 1) + 1])
                        broadcast_ids(k + 2)
                    if c >= VC - ACHUNKS[k]:
                        pe.wait_ge(onehot_act, ABEFORE[k + 1] - VC + c + 1)
                    for part in (table_hi, table_lo):
                        last = nc.tensor.matmul(table_bank[k][:, at:B], part[:, k % 2, c, :], onehot[:, k % 2, c, at:B],
                                                start=c == 0 and part is table_hi,
                                                stop=c == VC - 1 and part is table_lo)
                last.then_inc(table_done, 1)

            def transpose_group(n):
                t, g = n // NG, n % NG
                if n >= 2:
                    pe.wait_ge(group_used, n - 1)
                pe.wait_ge(rows_in[t][g], 16 * len([f for f in group_of(t, g) if f != DENSE]))
                for k, f in enumerate(group_of(t, g)):
                    if f == DENSE and t == 0:
                        pe.wait_ge(dense_in, 16)
                    src = dense_sb[:, t, :] if f == DENSE else rows[:, t % ROWB, GATHER.index(f), :]
                    last = nc.tensor.transpose(ps_tp[n % 2][:, k, :], src, ident[:, :])
                last.then_inc(group_done, 1)

            def gram_banks(t, banks):
                if banks[0] == 0:
                    pe.wait_ge(group_used, NG * (t + 1))
                    pe.wait_ge(table_used, FULL if t < LATER_T else NL)
                    if t == 0:
                        pe.wait_ge(pad_ready, 2)
                for g in banks:
                    n = t * GB + g
                    if n >= 2:
                        pe.wait_ge(gram_act, n - 1)
                        pe.wait_ge(gram_dve, n - 1)
                    for k in range(QB):
                        q = g * QB + k
                        last = nc.tensor.matmul(ps_gram[n % 2][0:GM, k * GW:(k + 1) * GW],
                                                featT[:, t, q, :, :].rearrange("d s f -> d (s f)")[:, 1:1 + GM],
                                                featT[:, t, q, :, 0:FJ], start=True, stop=True)
                    last.then_inc(gram_done, 1)

            def transpose_z(t):
                pe.wait_ge(z_done, (F - 1) * (t + 1))
                if t >= 1:
                    pe.wait_ge(zT_done, t)
                for c in range(ZC):
                    last = nc.tensor.transpose(ps_z[0:ZK, c, :], z[:, t % 2, c * ZK:(c + 1) * ZK], ident[:, :])
                last.then_inc(ztp_done, 1)

            def transpose_last_z(c):
                t = TILES - 1
                pe.wait_ge(z_act, APACK if c == 0 else APACK + APACK_MORE)
                if c >= 1:
                    packed = features_up_to(c) - APACK - APACK_MORE
                    pe.wait_ge(z_done, (F - 1) * t + min(packed, DPACK))
                    pe.wait_ge(zT_done, t)
                if c == ZC - 1:
                    pe.wait_ge(z_pool, PPACK)
                nc.tensor.transpose(last_z[c], z[:, t % 2, c * ZK:(c + 1) * ZK], ident[:, :]).then_inc(ztp_last, 1)

            def layer1_last_pairs(c):
                t = TILES - 1
                if c == 0:
                    pe.wait_ge(zT_first, 1)
                else:
                    pe.wait_ge(zT_done, t + c)
                for half in range(2):
                    for n in range(C1 // 2):
                        m = slice((half * C1 // 2 + n) * P, (half * C1 // 2 + n + 1) * P)
                        last = nc.tensor.matmul(ps_h1[half][:, n, :], w1z[:, c, m], zT[:, c, t % 2, :],
                                                start=False, stop=n == C1 // 2 - 1 and c == ZC - 1)
                    if c == ZC - 1:
                        last.then_inc(h1_done, 1)

            def layer1_dense(t, half):
                if t == 0:
                    pe.wait_ge(w1_in, 32)
                else:
                    pe.wait_ge(h1_relu, C1 * (t - 1) + C1 // 2 * (half + 1))
                for n in range(C1 // 2):
                    m = slice((half * C1 // 2 + n) * P, (half * C1 // 2 + n + 1) * P)
                    nc.tensor.matmul(ps_h1[half][:, n, :], w1d[:, m], denseT[:, t, :], start=n == 0, stop=False)

            def layer1(t, half):
                layer1_dense(t, half)
                pe.wait_ge(zT_done, t + 1)
                for n in range(C1 // 2):
                    m = slice((half * C1 // 2 + n) * P, (half * C1 // 2 + n + 1) * P)
                    for c in range(ZC):
                        last = nc.tensor.matmul(ps_h1[half][:, n, :], w1z[:, c, m], zT[:, c, t % 2, :],
                                                start=False, stop=n == C1 // 2 - 1 and c == ZC - 1)
                last.then_inc(h1_done, 1)

            def layer2(t, chunks=range(C1)):
                if t == 0:
                    pe.wait_ge(w2_in, 16)
                elif t < TILES - 1 and chunks[0] == 0:
                    pe.wait_ge(y_copied, t)
                for c in chunks:
                    pe.wait_ge(h1_relu, C1 * t + c + 1)
                    for n in range(C2):
                        last = nc.tensor.matmul(ps_h2[t][:, n, :], w2[:, c, n * P:(n + 1) * P], h1T[:, t % 2, c, :],
                                                start=c == 0 and n == 0, stop=c == C1 - 1 and n == C2 - 1)
                if chunks[-1] == C1 - 1:
                    last.then_inc(h2_done, 1)

            def layer3(t):
                pe.wait_ge(h2_relu, C2 * (t + 1))
                if t == 0:
                    pe.wait_ge(small_in, 48)
                for c in range(C2):
                    last = nc.tensor.matmul(ps_h2[t][0:1, C2, :], w3[:, c:c + 1], h2T[:, t % 2, c, :],
                                            start=c == 0, stop=c == C2 - 1)
                last.then_inc(y_done, 1)

            pe.wait_ge(consts_ready, 2)
            keep_busy(WARM[0])
            pe.wait_ge(consts_ready, 3)
            broadcast_ids(0)
            broadcast_ids(1)
            for t in range(TILES):
                last = nc.tensor.matmul(ps_h2[0][0:NTAB, t, :], ids_r[:, t, :], ident_r[:, :], start=True, stop=True)
            last.then_inc(idsT_done, 1)
            keep_busy(WARM[1])
            pe.wait_ge(ident_ready, 1)
            for k in range(NL):
                lookup(k)
                for n in AFTER_TABLE[k]:
                    transpose_group(n)
            at = 0
            for bank, n in zip(LATER_BANKS, LATER):
                gram_banks(0, range(at, bank))
                transpose_group(n)
                at = bank
            gram_banks(0, range(at, GB))
            gram_banks(1, range(0, 4))
            transpose_group(2 * NG)
            gram_banks(1, range(4, GB))
            transpose_z(0)
            transpose_group(2 * NG + 1)
            for t in range(2, TILES):
                for half in range(2):
                    layer1(t - 2, half)
                transpose_group(NG * t + AHEAD)
                transpose_z(t - 1)
                if t < TILES - 1:
                    transpose_group(NG * t + AHEAD + 1)
                    transpose_group(NG * t + AHEAD + 2)
                    layer2(t - 2, range(0, 2))
                    transpose_group(NG * t + NG - 1)
                    layer2(t - 2, range(2, C1))
                else:
                    layer2(t - 2)
                    layer1(t - 1, 0)
                    transpose_group(NG * t + AHEAD + 1)
                    layer3(t - 2)
                    layer1(t - 1, 1)
                    transpose_group(NG * t + AHEAD + 2)
                    transpose_group(NG * t + NG - 1)
                    layer2(t - 1, range(0, 2))
                gram_banks(t, range(0, 4))
                if t < TILES - 1:
                    layer3(t - 2)
                    transpose_group(NG * (t + 1))
                gram_banks(t, range(4, GB))
                if t < TILES - 1:
                    transpose_group(NG * (t + 1) + 1)
            t = TILES - 1
            for half in range(2):
                layer1_dense(t, half)
            layer2(t - 1, range(2, C1))
            transpose_last_z(0)
            transpose_last_z(1)
            layer1_last_pairs(0)
            transpose_last_z(2)
            layer1_last_pairs(1)
            layer1_last_pairs(2)
            layer2(t)
            layer3(t - 1)
            layer3(t)

        @block.scalar
        def _(act):
            def split_hi(k):
                act.wait_ge(raw_in[k % RAW], 32 * (k // RAW + 1))
                if k >= 2:
                    act.wait_ge(table_done, k - 1)
                nc.scalar.copy(table_hi[:, k % 2], table_raw[:, k % RAW]).then_inc(hi_done, 1)

            def away_at(k):
                return 0 if k % 2 == (FULL - 1) % 2 else ACHUNKS[FULL - 1]

            def write_away(k):
                act.wait_ge(ids_bc, k + 1)
                if k == 0:
                    act.wait_ge(onehot_dve, 2)
                if k >= 2:
                    act.wait_ge(onehot_act, ABEFORE[k - 1])
                t = first_tile(k)
                for a in range(ACHUNKS[k]):
                    c = VC - ACHUNKS[k] + a
                    nc.scalar.activation(away[:, away_at(k) + a, t * P:B],
                                         ps_h1[k % 2][0:VK, t:TILES, :].rearrange("k t p -> k (t p)"),
                                         ACT.Abs, scale=-1.0, bias=vnr[0:VK, c:c + 1]
                                         ).then_inc(away_done, 1)

            def write_onehot(k):
                if k >= 2:
                    act.wait_ge(table_done, k - 1)
                for a in range(ACHUNKS[k]):
                    act.wait_ge(away_done, ABEFORE[2] if k == 0 else ABEFORE[k] + a + 1)
                    at = first_tile(k) * P
                    nc.scalar.activation(onehot[:, k % 2, VC - ACHUNKS[k] + a, at:B], away[:, away_at(k) + a, at:B], ACT.Relu,
                                         scale=-1.0, bias=1.0).then_inc(onehot_act, 1)

            def copy_table(k):
                f = LOOKUP[k]
                act.wait_ge(table_done, k + 1)
                t = first_tile(k)
                nc.scalar.copy(featT[:, t:TILES, :, :, f].rearrange("d t q s -> d t s q"),
                               table_bank[k][:, t * P:B].rearrange("d (t s q) -> d t s q", s=SLOTS, q=S)
                               ).then_inc(table_used, 1)

            def copy_group(n):
                t, g = n // NG, n % NG
                act.wait_ge(group_done, n + 1)
                if DENSE in GROUPS[g]:
                    nc.scalar.copy(denseT[:, t, :], ps_tp[n % 2][:, GROUPS[g].index(DENSE), :])
                for k, f, m in runs(group_of(t, g)):
                    last = nc.scalar.copy(featT[:, t, :, :, f:f + m].rearrange("d q s f -> d f s q"),
                                          ps_tp[n % 2][:, k:k + m, :].rearrange("d f (s q) -> d f s q", q=S))
                last.then_inc(group_used, 1)

            def copy_gram(t, banks):
                if t >= 2:
                    act.wait_ge(gramT_done, 2 * (t - 1))
                for g in banks:
                    n = t * GB + g
                    act.wait_ge(gram_done, n + 1)
                    for s in (0, 1):
                        src = ps_gram[n % 2][s * S:(s + 1) * S, 0:QB * GW].rearrange(
                            "i (q s j) -> i s j q", q=QB, s=SLOTS)[:, s]
                        last = nc.scalar.copy(gram[s * S:(s + 1) * S, t % 2, :, g * QB:(g + 1) * QB], src)
                    last.then_inc(gram_act, 1)

            def pack_pairs(t, features):
                act.wait_ge(gramT_done, 2 * t + (1 if features[0] == 0 else 2))
                act.wait_ge(ztp_done, t - 1)
                for j in features:
                    at = j * (2 * F - j - 1) // 2
                    nc.scalar.copy(z[:, t % 2, at:at + F - 1 - j], gramT[:, j, j:FJ]).then_inc(z_act, 1)

            def relu1(t, half):
                if t == 0:
                    act.wait_ge(small_in, 48)
                act.wait_ge(h1_done, 2 * t + half + 1)
                for n in range(half * C1 // 2, (half + 1) * C1 // 2):
                    nc.scalar.activation(h1T[:, t % 2, n, :], ps_h1[n // 2][:, n % 2, :], ACT.Relu,
                                         bias=b1c[:, n:n + 1]).then_inc(h1_relu, 1)

            def relu2(t):
                act.wait_ge(h2_done, t + 1)
                for n in range(C2):
                    nc.scalar.activation(h2T[:, t % 2, n, :], ps_h2[t][:, n, :], ACT.Relu,
                                         bias=b2c[:, n:n + 1]).then_inc(h2_relu, 1)

            act.wait_ge(consts_ready, 1)
            nc.scalar.activation(away[:, 0, 0:VC], vnr[0:VK, :], ACT.Abs).then_inc(warm_done, 1)
            act.wait_ge(warm_done, 1)
            act.wait_ge(pad_ready, 1)
            nc.scalar.copy(featT[:, TILES // 2:TILES, :, 0:SLOTS - 1, F:S],
                           featT[:, 0:TILES // 2, :, 0:SLOTS - 1, F:S]).then_inc(pad_ready, 1)
            act.wait_ge(consts_ready, 3)
            split_hi(0)
            write_away(1)
            split_hi(1)
            write_away(0)
            write_onehot(0)
            for k in range(1, NL):
                write_onehot(k)
                if k == 1:
                    act.wait_ge(idsT_done, 1)
                    nc.scalar.copy(idsT[:, :], ps_h2[0][0:NTAB, :, :].rearrange("f t p -> f (t p)")
                                   ).then_inc(idsT_ready, 1)
                if k + 1 < NL:
                    write_away(k + 1)
                    split_hi(k + 1)
                copy_table(k - 1)
                for n in AFTER_TABLE[k - 1]:
                    copy_group(n)
            copy_table(NL - 1)
            for n in AFTER_TABLE[NL - 1]:
                copy_group(n)
            at = 0
            for bank, n in zip(LATER_BANKS, LATER):
                copy_gram(0, range(at, bank))
                copy_group(n)
                at = bank
            copy_gram(0, range(at, GB))
            copy_gram(1, range(0, 4))
            copy_group(2 * NG)
            copy_gram(1, range(4, GB))
            copy_group(2 * NG + 1)
            for t in range(2, TILES):
                for half in range(2):
                    relu1(t - 2, half)
                copy_group(NG * t + AHEAD)
                if t == TILES - 1:
                    relu2(t - 2)
                    relu1(t - 1, 0)
                copy_group(NG * t + AHEAD + 1)
                if t == TILES - 1:
                    relu1(t - 1, 1)
                for g in range(AHEAD + 2, NG):
                    copy_group(NG * t + g)
                if t < TILES - 1:
                    relu2(t - 2)
                copy_gram(t, range(0, 4))
                if t < TILES - 1:
                    copy_group(NG * (t + 1))
                copy_gram(t, range(4, GB))
                if t < TILES - 1:
                    copy_group(NG * (t + 1) + 1)
            t = TILES - 1
            pack_pairs(t, range(APACK))
            pack_pairs(t, range(APACK, APACK + APACK_MORE))
            act.wait_ge(ztp_last, 1)
            act.wait_ge(h1_done, 2 * (t - 1))
            nc.scalar.copy(zT[:, 0, t % 2, :], last_z[0]).then_inc(zT_first, 1)
            relu2(t - 1)
            relu1(t, 0)
            relu1(t, 1)
            relu2(t)

        @block.vector
        def _(dve):
            def split_lo(k):
                dve.wait_ge(hi_done, k + 1)
                if k >= 2:
                    dve.wait_ge(table_done, k - 1)
                nc.vector.tensor_tensor(table_lo[:, k % 2], table_raw[:, k % RAW], table_hi[:, k % 2].bitcast(fp32),
                                        ALU.subtract).then_inc(lo_done, 1)

            def write_onehot(k, starts):
                if k == 0:
                    dve.wait_ge(ids_bc, 1)
                else:
                    dve.wait_ge(away_done, ABEFORE[k + 1] if k >= 2 else ACHUNKS[1])
                if k >= 2:
                    dve.wait_ge(table_done, k - 1)
                t = first_tile(k)
                for c in starts:
                    end = VD if c == 0 else VC - ACHUNKS[k]
                    part = [VK, end - c, B - t * P]
                    nc.vector.tensor_tensor(
                        onehot[:, k % 2, c:end, t * P:B],
                        ps_h1[k % 2][0:VK, t:TILES, :].rearrange("k t (o p) -> k o (t p)", o=1).broadcast_to(part),
                        vnr[0:VK, c:end].rearrange("k (c o) -> k c o", o=1).broadcast_to(part),
                        ALU.is_equal).then_inc(onehot_dve, 1)

            def copy_gram(t, banks):
                for g in banks:
                    n = t * GB + g
                    dve.wait_ge(gram_done, n + 1)
                    if g == 0 and t >= 2:
                        dve.wait_ge(gramT_done, 2 * (t - 1))
                    if n == 0:
                        dve.wait_ge(rim_ready, 1)
                    for s in (2, 3):
                        rows_of = slice(s * S, min((s + 1) * S, GM))
                        src = ps_gram[n % 2][rows_of, 0:QB * GW].rearrange(
                            "i (q s j) -> i s j q", q=QB, s=SLOTS)[:, s]
                        last = nc.vector.tensor_copy(gram[rows_of, t % 2, :, g * QB:(g + 1) * QB], src)
                    last.then_inc(gram_dve, 1)

            def transpose_gram(t, part):
                low, high = (0, APACK) if part == 0 else (APACK, FJ)
                dve.wait_ge(gram_act, (t + 1) * GB)
                dve.wait_ge(gram_dve, (t + 1) * GB)
                if t >= 1:
                    dve.wait_ge(z_done, (F - 1) * t)
                nc.vector.transpose(gramT[:, low:high, :].rearrange("b j i -> b (j i)"),
                                    gram[:, t % 2, low:high, :].rearrange("p j q -> p (j q)")).then_inc(gramT_done, 1)

            def pack_pairs(t, features):
                dve.wait_ge(gramT_done, 2 * (t + 1))
                if t >= 2:
                    dve.wait_ge(ztp_done, t - 1)
                for j in features:
                    at = j * (2 * F - j - 1) // 2
                    nc.vector.tensor_copy(z[:, t % 2, at:at + F - 1 - j], gramT[:, j, j:FJ]).then_inc(z_done, 1)

            def copy_zT(t):
                dve.wait_ge(ztp_done, t + 1)
                if t >= 2:
                    dve.wait_ge(h1_done, 2 * (t - 1))
                nc.vector.tensor_copy(zT[:, :, t % 2, :], ps_z[0:ZK, 0:ZC, :]).then_inc(zT_done, 1)

            def copy_last_zT(c):
                t = TILES - 1
                dve.wait_ge(ztp_last, c + 1)
                dve.wait_ge(h1_done, 2 * (t - 1))
                nc.vector.tensor_copy(zT[:, c, t % 2, :], last_z[c]).then_inc(zT_done, 1)

            def copy_y(t):
                dve.wait_ge(y_done, t + 1)
                nc.vector.tensor_copy(y_row[:, :, t], ps_h2[t][0:1, C2, :]).then_inc(y_copied, 1)

            dve.wait_ge(vnr_ready, 1)
            nc.vector.tensor_copy(vnr[:, :], vnr_i[:, :]).then_inc(consts_ready, 1)
            dve.wait_ge(ident_ready, 1)
            nc.vector.tensor_copy(ident_r[:, :], ident[:, :]).then_inc(consts_ready, 1)
            nc.vector.memset(featT[:, 0:TILES // 2, :, 0:SLOTS - 1, F:S], 0.0).then_inc(pad_ready, 1)
            dve.wait_ge(ids_in, 16)
            nc.vector.tensor_copy(ids_r[:, :, :], ids_sb[:, :, :]).then_inc(consts_ready, 1)
            dve.wait_ge(consts_ready, 3)
            write_onehot(0, [0, VD])
            split_lo(0)
            for k in range(1, NL):
                write_onehot(k, [0])
                split_lo(k)
                write_onehot(k, [VD])
            copy_gram(0, range(GB))
            transpose_gram(0, 0)
            copy_gram(1, range(0, 1))
            transpose_gram(0, 1)
            copy_gram(1, range(1, 2))
            pack_pairs(0, range(0, 8))
            copy_gram(1, range(2, 3))
            pack_pairs(0, range(8, 17))
            copy_gram(1, range(3, 4))
            pack_pairs(0, range(17, F - 1))
            copy_gram(1, range(4, GB))
            copy_zT(0)
            for part in range(2):
                transpose_gram(1, part)
            pack_pairs(1, range(F - 1))
            for t in range(2, TILES):
                copy_zT(t - 1)
                if t == TILES - 1:
                    copy_y(t - 2)
                copy_gram(t, range(0, 5))
                if t < TILES - 1:
                    copy_y(t - 2)
                copy_gram(t, range(5, GB))
                for part in range(2):
                    transpose_gram(t, part)
                pack_pairs(t, range(F - 1) if t < TILES - 1 else range(APACK + APACK_MORE, F - 1 - PPACK))
            copy_last_zT(1)
            copy_last_zT(2)
            copy_y(TILES - 2)
            copy_y(TILES - 1)


_INS = ["r_dense_x", "ids"] + [f"tbl_{i}" for i in range(NTAB)] + ["W_top1", "b_top1", "W_top2", "b_top2", "W_top3"]


def kernel(**inputs):
    import numpy as _np
    import concourse.bacc as _bacc
    from concourse import mybir as _mybir
    from concourse.bass_utils import run_bass_kernel_spmd as _run

    nc = _bacc.Bacc("TRN2", target_bir_lowering=False, num_devices=1)
    arrays, aps = {}, []
    for name in _INS:
        a = _np.ascontiguousarray(inputs[name])
        arrays[f"in_{name}"] = a
        aps.append(nc.dram_tensor(f"in_{name}", a.shape, _mybir.dt.from_np(a.dtype), kind="ExternalInput").ap())
    y = nc.dram_tensor("out_y", (B, 1), _mybir.dt.float32, kind="ExternalOutput").ap()
    dense, ids = aps[0:2]
    W1, b1, W2, b2, W3 = aps[2 + NTAB:]
    build(nc, dense, ids, aps[2:2 + NTAB], W1, b1, W2, b2, W3, y)
    r = _run(nc, [arrays], core_ids=[0])
    return r.results[0]["out_y"]
```
